# Optimizing a Trainium2 kernel written in Bass

```python
import numpy as np
import jax
import jax.numpy as jnp

def _softmax(x, axis=-1):
    return jax.nn.softmax(x, axis=axis)

def _gelu(x):
    return jax.nn.gelu(x, approximate=True)

def _silu(x):
    return jax.nn.silu(x)

def _sigmoid(x):
    return jax.nn.sigmoid(x)

def _layernorm(x, axis=-1, eps=1e-05):
    m = jnp.mean(x, axis=axis, keepdims=True)
    v = jnp.var(x, axis=axis, keepdims=True)
    return (x - m) / jnp.sqrt(v + eps)

def _scatter_add(tgt, idx, src, axis=0):
    return tgt.at[idx].add(src)

def _segment_sum(src, seg, n):
    return jax.ops.segment_sum(src, seg, n)
kernel_name = 'mk_conv_seq_d1_conv_nchw256_r4_248427'

def setup_inputs(seed: int=0):
    np.random.seed(seed)
    _w = jnp.asarray

    def _rec_inputs():
        import jax
        import jax.numpy as jnp
        _gk = jax.random.key(seed)
        x = 7.22e-05 + 1 * jax.random.normal(jax.random.fold_in(_gk, 1), (8, 64, 16, 16), jnp.float32)
        return x
    x = _rec_inputs()

    def _L0_conv_setup():
        import jax, jax.numpy as jnp
        import numpy as np
        EPS = 1e-05
        GROUPS = 32

        def group_norm(x, w, b):
            B, C, H, W = x.shape
            g = GROUPS
            xr = x.reshape(B, g, C // g, H * W)
            mean = xr.mean(axis=(2, 3), keepdims=True)
            var = xr.var(axis=(2, 3), keepdims=True)
            h = ((xr - mean) / jnp.sqrt(var + EPS)).reshape(B, C, H, W)
            return h * w[None, :, None, None] + b[None, :, None, None]
        key = jax.random.key(seed)
        ks = jax.random.split(key, 7)
        B, C, H, W = (8, 64, 16, 16)
        d = C // 8
        x = jax.random.normal(ks[0], (B, C, H, W), dtype=jnp.float32)
        norm_w = 1.0 + 0.1 * jax.random.normal(ks[1], (C,), dtype=jnp.float32)
        norm_b = 0.1 * jax.random.normal(ks[2], (C,), dtype=jnp.float32)
        s = 1.0 / np.sqrt(C)
        Wq = jax.random.normal(ks[3], (d, C), dtype=jnp.float32) * s
        Wk = jax.random.normal(ks[4], (d, C), dtype=jnp.float32) * s
        Wv = jax.random.normal(ks[5], (C, C), dtype=jnp.float32) * s
        Wproj = jax.random.normal(ks[6], (C, C), dtype=jnp.float32) * s
        gamma = jnp.full((1,), 0.5, dtype=jnp.float32)
        return {'x': x, 'norm_w': norm_w, 'norm_b': norm_b, 'Wq': Wq, 'Wk': Wk, 'Wv': Wv, 'Wproj': Wproj, 'gamma': gamma}
    _L0_conv_all = _L0_conv_setup()
    _L0_conv_in = {k: v for k, v in _L0_conv_all.items() if k in ('norm_w', 'norm_b', 'Wq', 'Wk', 'Wv', 'Wproj', 'gamma')}
    del _L0_conv_all
    return {'x': x, 'L0_conv_norm_w': _L0_conv_in['norm_w'], 'L0_conv_norm_b': _L0_conv_in['norm_b'], 'L0_conv_Wq': _L0_conv_in['Wq'], 'L0_conv_Wk': _L0_conv_in['Wk'], 'L0_conv_Wv': _L0_conv_in['Wv'], 'L0_conv_Wproj': _L0_conv_in['Wproj'], 'L0_conv_gamma': _L0_conv_in['gamma']}

def reference(x, L0_conv_norm_w, L0_conv_norm_b, L0_conv_Wq, L0_conv_Wk, L0_conv_Wv, L0_conv_Wproj, L0_conv_gamma):
    import jax
    import jax.numpy as jnp

    def _L0_conv_ref(x, norm_w, norm_b, Wq, Wk, Wv, Wproj, gamma):
        import jax, jax.numpy as jnp
        import numpy as np
        EPS = 1e-05
        GROUPS = 32

        def group_norm(x, w, b):
            B, C, H, W = x.shape
            g = GROUPS
            xr = x.reshape(B, g, C // g, H * W)
            mean = xr.mean(axis=(2, 3), keepdims=True)
            var = xr.var(axis=(2, 3), keepdims=True)
            h = ((xr - mean) / jnp.sqrt(var + EPS)).reshape(B, C, H, W)
            return h * w[None, :, None, None] + b[None, :, None, None]
        B, C, H, W = x.shape
        N = H * W
        h = group_norm(x, norm_w, norm_b)
        hf = h.reshape(B, C, N)
        d = Wq.shape[0]
        q = jnp.einsum('dc,bcn->bnd', Wq, hf)
        k = jnp.einsum('dc,bcn->bdn', Wk, hf)
        v = jnp.einsum('oc,bcn->bno', Wv, hf)
        scale = d ** (-0.5)
        attn = jax.nn.softmax(jnp.einsum('bnd,bdm->bnm', q, k) * scale, axis=-1)
        out = jnp.einsum('bnm,bmo->bno', attn, v)
        out = out.transpose(0, 2, 1).reshape(B, C, H, W)
        proj = jnp.einsum('oc,bchw->bohw', Wproj, out)
        return x + gamma[0] * proj

    def _gn(v, G=32, eps=1e-05):
        B_, C_, H_, W_ = v.shape
        g = v.reshape(B_, G, C_ // G, H_, W_)
        m = jnp.mean(g, axis=(2, 3, 4), keepdims=True)
        s = jnp.var(g, axis=(2, 3, 4), keepdims=True)
        return ((g - m) / jnp.sqrt(s + eps)).reshape(v.shape)

    def _ln_c(v, eps=1e-06):
        m = jnp.mean(v, axis=1, keepdims=True)
        s = jnp.var(v, axis=1, keepdims=True)
        return (v - m) / jnp.sqrt(s + eps)

    def _ln_t(v, eps=1e-05):
        m = jnp.mean(v, axis=-1, keepdims=True)
        s = jnp.var(v, axis=-1, keepdims=True)
        return (v - m) / jnp.sqrt(s + eps)

    def _to_tokens(v):
        B_, C_, H_, W_ = v.shape
        return v.reshape(B_, C_, H_ * W_).transpose(0, 2, 1)

    def _from_tokens(t, like):
        B_, C_, H_, W_ = like.shape
        return t.transpose(0, 2, 1).reshape(B_, C_, H_, W_)
    x = _L0_conv_ref(x, L0_conv_norm_w, L0_conv_norm_b, L0_conv_Wq, L0_conv_Wk, L0_conv_Wv, L0_conv_Wproj, L0_conv_gamma)
    return x

_drawn_inputs = setup_inputs


def setup_inputs(seed=0):
    import zlib

    import numpy as np

    out = dict(_drawn_inputs(seed))
    spreads = {}
    factors = {'L0_conv_norm_w': 2.878}
    for name, (base, spread) in spreads.items():
        noise = np.random.default_rng([zlib.crc32(name.encode()), seed]).standard_normal(out[name].shape)
        drawn = base * np.exp(spread * noise) if base else spread * noise
        out[name] = jnp.asarray(drawn.astype(out[name].dtype))
    for name, factor in factors.items():
        out[name] = (out[name] * factor).astype(out[name].dtype)
    return out
```

```python
from contextlib import ExitStack

import concourse.bass as bass
from concourse import mybir

ALU = mybir.AluOpType
ACT = mybir.ActivationFunctionType
AX_X = mybir.AxisListType.X
F32 = mybir.dt.float32
F32R = mybir.dt.float32r
BF16 = mybir.dt.bfloat16

B, C, HH, WW = 8, 64, 16, 16
N = HH * WW
GROUPS = 32
CPG = C // GROUPS
D = C // 8
EPS = 1e-5
SCALE = float(D) ** -0.5
P = 128
PAIRS = B // 2
QUADS = B // 4
PARTS = 4
ROWS = PARTS * D
NH = N // P
UW = C + 2

A_NORM_W, A_NORM_B, A_QMASK, A_KMASK, A_WQ, A_WK = 0, 1, 2, 3, 4, 4 + 2 * ROWS
A_COLS = 4 + 4 * ROWS
B_WV, B_WPROJ, B_GAMMA = 0, P, 2 * P
B_COLS = 2 * P + 1

WARM = 10


def build_attention(nc, x, pack_a, pack_b, out):
    x_pairs = x.rearrange("(j s) c n -> j (s c) n", s=2)
    out_pairs = out.rearrange("(j s) c n -> j (s c) n", s=2)

    with ExitStack() as ctx:
        def sb(name, shape, dt=F32):
            return ctx.enter_context(nc.sbuf_tensor(name, shape, dt))

        def bank(name):
            return ctx.enter_context(nc.psum_tensor(name, [P, 512], F32))

        def sem(name):
            return ctx.enter_context(nc.semaphore(name))

        X = sb("X", [P, PAIRS, N])
        A = sb("A", [P, A_COLS])
        Bp = sb("Bp", [P, B_COLS])
        zeros = sb("zeros", [P, 512], BF16)
        neg_half_g = sb("neg_half_g", [P, P])
        dev_g = sb("dev_g", [P, P])
        ident = sb("ident", [P, P])
        ident_r = sb("ident_r", [P, P], F32R)
        neg_eps = sb("neg_eps", [1, P])
        var_cols = sb("var_cols", [1, 4])
        neg_ones = sb("neg_ones", [P, P], F32R)
        exponent = sb("exponent", [P, 2])
        warm_exp = sb("warm_exp", [P, 1])
        stats = sb("stats", [P, PAIRS, 6])
        mv = sb("mv", [P, PAIRS, 2])
        var = sb("var", [P, PAIRS])
        rstd = sb("rstd", [P, PAIRS])
        mul = sb("mul", [P, PAIRS])
        add = sb("add", [P, PAIRS])
        H = sb("H", [P, PAIRS, N])
        WU = sb("WU", [P, P])
        QKhi = sb("QKhi", [P, QUADS, 2 * N], F32R)
        Qs = sb("Qs", [P, QUADS, N], F32R)
        Ks = sb("Ks", [P, QUADS, N], F32R)
        U = sb("U", [P, PAIRS, NH, 2, UW])
        mx = sb("mx", [P, PAIRS, 2, NH])
        MXC = sb("MXC", [P, PAIRS, NH, P], F32R)
        MXT = sb("MXT", [P, PAIRS, N], F32R)
        E = sb("E", [P, B, NH, N])
        rec = sb("rec", [P, PAIRS, NH * 2])
        Z = sb("Z", [P, PAIRS, NH, 2, C])
        Y = sb("Y", [P, PAIRS, N])

        bank_qk = [bank("qk0"), bank("qk1")]
        bank_m = bank("bank_m")
        bank_u = bank("bank_u")
        bank_st = [bank("st0"), bank("st1")]
        bank_s = [bank("s0"), bank("s1")]
        bank_gn = bank_st[1]
        bank_pv = [bank_qk[0], bank_u]
        bank_t = bank_qk[1]

        x_in = [sem(f"x_in{j}") for j in range(PAIRS)]
        a_in, b_in = sem("a_in"), sem("b_in")
        zeros_set, mxc_zeroed, neg_g_set, ident_set = sem("zeros_set"), sem("mxc_zeroed"), sem("neg_g_set"), sem("ident_set")
        eps_set, exponent_set, dev_set, identr_set = sem("eps_set"), sem("exponent_set"), sem("dev_set"), sem("identr_set")
        ones_set, pool_chain = sem("ones_set"), sem("pool_chain")
        stats_done, mv_done, group_stats = sem("stats_done"), sem("mv_done"), sem("group_stats")
        var_done, rstd_done, mul_done, add_done = sem("var_done"), sem("rstd_done"), sem("mul_done"), sem("add_done")
        h_dve, h_act = sem("h_dve"), sem("h_act")
        wu_ready, wu_kept = sem("wu_ready"), sem("wu_kept")
        qk_ready, qk_high, qk_stacked = sem("qk_ready"), sem("qk_high"), sem("qk_stacked")
        u_ready, u_kept = sem("u_ready"), sem("u_kept")
        s_ready, max_done, max_high, max_cols = sem("s_ready"), sem("max_done"), sem("max_high"), sem("max_cols")
        max_turned, max_rows = sem("max_turned"), sem("max_rows")
        st_ready, exp_done = sem("st_ready"), sem("exp_done")
        pv_ready, rec_done, z_done = sem("pv_ready"), sem("rec_done"), sem("z_done")
        turned, y_done, y_out = sem("turned"), sem("y_done"), sem("y_out")

        block = ctx.enter_context(nc.Block())

        @block.sync
        def _(sp):
            for j in range(PAIRS):
                sp.dma_start(X[:, j, :], x_pairs[j]).then_inc(x_in[j], 16)
            for j in range(PAIRS):
                sp.wait_ge(y_done, j + 1)
                sp.dma_start(out_pairs[j], Y[:, j, :]).then_inc(y_out, 16)
            sp.wait_ge(y_out, 16 * PAIRS)

        @block.gpsimd
        def _(pool):
            nc.gpsimd.memset(ident[:], 0.0).then_inc(pool_chain, 1)
            nc.gpsimd.memset(neg_half_g[:], -1.0 / CPG).then_inc(pool_chain, 1)
            pool.wait_ge(pool_chain, 1)
            nc.gpsimd.affine_select(out=ident[:], in_=ident[:], compare_op=ALU.not_equal, fill=1.0, base=0,
                                    pattern=[[-1, P]], channel_multiplier=1).then_inc(ident_set, 1)
            blocks = neg_half_g[:].rearrange("p (g c) -> p g c", c=CPG)
            pool.wait_ge(pool_chain, 2)
            nc.gpsimd.affine_select(out=blocks, in_=blocks, compare_op=ALU.is_ge, fill=0.0, base=0,
                                    pattern=[[-CPG, P // CPG], [0, CPG]], channel_multiplier=1).then_inc(pool_chain, 1)
            pool.wait_ge(pool_chain, 3)
            nc.gpsimd.affine_select(out=blocks, in_=blocks, compare_op=ALU.is_ge, fill=0.0, base=CPG - 1,
                                    pattern=[[CPG, P // CPG], [0, CPG]], channel_multiplier=-1).then_inc(neg_g_set, 1)
            nc.gpsimd.memset(exponent[:], -0.5).then_inc(exponent_set, 1)
            nc.gpsimd.memset(neg_ones[:].bitcast(F32), -1.0).then_inc(ones_set, 1)
            nc.gpsimd.memset(MXC[:].rearrange("p j h c -> p (j h c)").bitcast(F32), 0.0).then_inc(mxc_zeroed, 1)
            for j in range(PAIRS):
                nc.gpsimd.memset(U[:, j, :, :, C:UW].rearrange("p h s c -> p (h s) c"), 1.0).then_inc(ones_set, 1)
            pool.wait_ge(exponent_set, 1)
            for q in range(QUADS):
                two = slice(2 * q, 2 * q + 2)
                pool.wait_ge(var_done, 2 * (q + 1))
                nc.gpsimd.tensor_tensor(rstd[:, two], var[:, two], exponent[:], ALU.pow).then_inc(rstd_done, 1)

        @block.scalar
        def _(act):
            act.dma_start(A[:], pack_a).then_inc(a_in, 16)
            act.dma_start(Bp[:], pack_b).then_inc(b_in, 16)
            act.wait_ge(zeros_set, 1)
            nc.scalar.activation(warm_exp[:], zeros[:, 0:1], ACT.Exp)

            def keep_high(q):
                act.wait_ge(qk_ready, q + 1)
                nc.scalar.copy(QKhi[:, q, :], bank_qk[q][:]).then_inc(qk_high, 1)

            def norm_odd(q):
                j = 2 * q + 1
                act.wait_ge(add_done, 2 * (q + 1))
                act.wait_ge(x_in[j], 16)
                nc.scalar.activation(H[:, j, :], X[:, j, :], ACT.Identity, bias=add[:, j:j + 1],
                                     scale=mul[:, j:j + 1]).then_inc(h_act, 1)

            def keep_u(q):
                act.wait_ge(u_ready, q + 1)
                dst = U[:, 2 * q:2 * q + 2, :, :, 0:C].rearrange("p j h s c -> p (j h s) c")
                nc.scalar.copy(dst, bank_u[:].rearrange("p (g c) -> p g c", c=C)).then_inc(u_kept, 1)

            def keep_max_rows(p):
                act.wait_ge(max_turned, p + 1)
                half = (p % 2) * N
                nc.scalar.copy(MXT[:, p, :], bank_m[:, half:half + N]).then_inc(max_rows, 1)

            def exps(b):
                act.wait_ge(st_ready, b + 1)
                nc.scalar.activation(E[:, b, :, :].rearrange("p h n -> p (h n)"), bank_st[b % 2][:], ACT.Exp,
                                     scale=SCALE).then_inc(exp_done, 1)

            norm_odd(0)
            keep_high(0)
            norm_odd(1)
            keep_u(0)
            keep_high(1)
            keep_u(1)
            for p in range(PAIRS):
                keep_max_rows(p)
                exps(2 * p)
                exps(2 * p + 1)

        @block.vector
        def _(dve):
            nc.vector.memset(zeros[:], 0.0).then_inc(zeros_set, 1)
            nc.vector.memset(neg_eps[:], -EPS).then_inc(eps_set, 1)
            nc.vector.memset(var_cols[:], 0.0).then_inc(eps_set, 1)
            dve.wait_ge(eps_set, 2)
            nc.vector.memset(var_cols[:, 1:4:2], 1.0).then_inc(eps_set, 1)
            dve.wait_ge(ident_set, 1)
            nc.vector.tensor_copy(ident_r[:], ident[:]).then_inc(identr_set, 1)
            dve.wait_ge(neg_g_set, 1)
            nc.vector.tensor_tensor(dev_g[:], ident[:], neg_half_g[:], ALU.add).then_inc(dev_set, 1)

            def channel_stats(q):
                for j in (2 * q, 2 * q + 1):
                    dve.wait_ge(x_in[j], 16)
                    nc.vector.bn_stats(stats[:, j, :], X[:, j, :]).then_inc(stats_done, 1)
                for j in (2 * q, 2 * q + 1):
                    dve.wait_ge(stats_done, j + 1)
                    nc.vector.bn_aggr(mv[:, j, :], stats[:, j, :]).then_inc(mv_done, 1)

            def group_var(q):
                dve.wait_ge(group_stats, q + 1)
                g = 8 * q
                for i in range(2):
                    j = 2 * q + i
                    nc.vector.tensor_scalar(var[:, j:j + 1], bank_gn[:, g + 4 + i:g + 5 + i], bank_gn[:, g + 4 + i:g + 5 + i],
                                            bank_gn[:, g + 2 * i + 1:g + 2 * i + 2], ALU.mult,
                                            ALU.subtract).then_inc(var_done, 1)

            def affine(q):
                two = slice(2 * q, 2 * q + 2)
                g = 8 * q
                dve.wait_ge(rstd_done, q + 1)
                if q == 0:
                    dve.wait_ge(a_in, 16)
                nc.vector.tensor_scalar(mul[:, two], rstd[:, two], A[:, A_NORM_W:A_NORM_W + 1], None,
                                        ALU.mult).then_inc(mul_done, 1)
                dve.wait_ge(mul_done, q + 1)
                for i in range(2):
                    j = 2 * q + i
                    nc.vector.tensor_scalar(add[:, j:j + 1], bank_gn[:, g + 2 * i:g + 2 * i + 1], mul[:, j:j + 1],
                                            A[:, A_NORM_B:A_NORM_B + 1], ALU.mult, ALU.add).then_inc(add_done, 1)
                j = 2 * q
                dve.wait_ge(add_done, 2 * q + 1)
                nc.vector.tensor_scalar(H[:, j, :], X[:, j, :], mul[:, j:j + 1], add[:, j:j + 1], ALU.mult,
                                        ALU.add).then_inc(h_dve, 1)

            def keep_wu():
                dve.wait_ge(wu_ready, 1)
                nc.vector.tensor_scalar(WU[:], bank_m[:, 0:P], Bp[:, B_GAMMA:B_GAMMA + 1], None,
                                        ALU.mult).then_inc(wu_kept, 1)

            def stack(q):
                dve.wait_ge(qk_high, q + 1)
                for t, (dst, mask) in enumerate(((Qs, A_QMASK), (Ks, A_KMASK))):
                    cols = slice(t * N, (t + 1) * N)
                    nc.vector.scalar_tensor_tensor(out=dst[:, q, :], in0=QKhi[:, q, cols].bitcast(F32),
                                                   scalar=A[:, mask:mask + 1], in1=bank_qk[q][:, cols],
                                                   op0=ALU.mult, op1=ALU.add).then_inc(qk_stacked, 1)

            def row_max(b):
                dve.wait_ge(s_ready, b + 1)
                nc.vector.tensor_reduce(mx[:, b // 2, b % 2, :], bank_s[b % 2][:].rearrange("p (h m) -> p h m", h=NH),
                                        AX_X, ALU.max).then_inc(max_done, 1)

            def split_max(p):
                r = 2 * ROWS * (p % 2)
                high = MXC[:, p, :, r:r + ROWS + 1:ROWS].rearrange("p h s -> p s h")
                low = MXC[:, p, :, r + 1:r + ROWS + 2:ROWS].rearrange("p h s -> p s h")
                if p == 0:
                    dve.wait_ge(mxc_zeroed, 1)
                dve.wait_ge(max_done, 2 * p + 2)
                nc.vector.tensor_copy(high, mx[:, p, :, :]).then_inc(max_high, 1)
                dve.wait_ge(max_high, p + 1)
                nc.vector.tensor_tensor(low, mx[:, p, :, :], high.bitcast(F32), ALU.subtract).then_inc(max_cols, 1)

            def normalize(p):
                dve.wait_ge(pv_ready, p + 1)
                pv = bank_pv[p % 2][:].rearrange("p (g c) -> p g c", c=P)
                nc.vector.reciprocal(rec[:, p, :].unsqueeze(2), pv[:, :, C:C + 1]).then_inc(rec_done, 1)
                dve.wait_ge(rec_done, p + 1)
                nc.vector.tensor_tensor(Z[:, p, :, :, :].rearrange("p h s c -> p (h s) c"), pv[:, :, 0:C],
                                        rec[:, p, :].unsqueeze(2).to_broadcast([P, NH * 2, C]),
                                        ALU.mult).then_inc(z_done, 1)

            def residual(p):
                dve.wait_ge(turned, p + 1)
                half = (p % 2) * N
                nc.vector.tensor_tensor(Y[:, p, :], bank_t[:, half:half + N], X[:, p, :], ALU.add).then_inc(y_done, 1)

            channel_stats(0)
            group_var(0)
            affine(0)
            channel_stats(1)
            keep_wu()
            group_var(1)
            stack(0)
            affine(1)
            row_max(0)
            row_max(1)
            stack(1)
            split_max(0)
            for p in range(1, PAIRS):
                row_max(2 * p)
                row_max(2 * p + 1)
                split_max(p)
                normalize(p - 1)
                residual(p - 1)
            normalize(PAIRS - 1)
            residual(PAIRS - 1)

        @block.tensor
        def _(pe):
            pe.wait_ge(zeros_set, 1)
            for _ in range(WARM):
                nc.tensor.matmul(bank_m[:], zeros[:, 0:P], zeros[:], start=True, stop=True)

            def weights_u():
                pe.wait_ge(b_in, 16)
                nc.tensor.matmul(bank_m[:, 0:P], Bp[:, B_WV:B_WV + P], Bp[:, B_WPROJ:B_WPROJ + P], start=True,
                                 stop=True).then_inc(wu_ready, 1)

            def group_stats_of(q):
                g = 8 * q
                if q == 0:
                    pe.wait_ge(eps_set, 3)
                    pe.wait_ge(neg_g_set, 1)
                    pe.wait_ge(dev_set, 1)
                nc.tensor.matmul(bank_gn[:, g:g + 4], neg_eps[:], var_cols[:], start=True, stop=False)
                pe.wait_ge(mv_done, 2 * q + 2)
                two = mv[:, 2 * q:2 * q + 2, :]
                nc.tensor.matmul(bank_gn[:, g:g + 4], neg_half_g[:], two.rearrange("p j t -> p (j t)"), start=False,
                                 stop=True)
                nc.tensor.matmul(bank_gn[:, g + 4:g + 6], dev_g[:], two[:, :, 0], start=True,
                                 stop=True).then_inc(group_stats, 1)

            def project_qk(q):
                if q == 0:
                    pe.wait_ge(a_in, 16)
                pe.wait_ge(h_dve, q + 1)
                for i, j in enumerate((2 * q, 2 * q + 1)):
                    if i == 1:
                        pe.wait_ge(h_act, q + 1)
                    for t, w in enumerate((A_WQ, A_WK)):
                        mm = nc.tensor.matmul(bank_qk[q][2 * ROWS * i:2 * ROWS * (i + 1), t * N:(t + 1) * N],
                                              A[:, w:w + 2 * ROWS], H[:, j, :], start=True, stop=True)
                mm.then_inc(qk_ready, 1)

            def project_u(q):
                if q == 0:
                    pe.wait_ge(wu_kept, 1)
                else:
                    pe.wait_ge(u_kept, q)
                for i, j in enumerate((2 * q, 2 * q + 1)):
                    for h in range(NH):
                        k = (i * NH + h) * P
                        mm = nc.tensor.matmul(bank_u[:, k:k + P], H[:, j, h * P:(h + 1) * P], WU[:], start=True,
                                              stop=True)
                mm.then_inc(u_ready, 1)

            def scores_by_query(b):
                if b % 4 == 0:
                    pe.wait_ge(qk_stacked, 2 * (b // 4) + 2)
                if b >= 2:
                    pe.wait_ge(max_done, b - 1)
                r = ROWS * (b % 4)
                for h in range(NH):
                    mm = nc.tensor.matmul(bank_s[b % 2][:, h * N:(h + 1) * N], Qs[r:r + ROWS, b // 4, h * P:(h + 1) * P],
                                          Ks[r:r + ROWS, b // 4, :], start=True, stop=True)
                mm.then_inc(s_ready, 1)

            def turn_max(p):
                if p == 0:
                    pe.wait_ge(identr_set, 1)
                else:
                    pe.wait_ge(max_rows, p)
                pe.wait_ge(max_cols, p + 1)
                half = (p % 2) * N
                for h in range(NH):
                    mm = nc.tensor.matmul(bank_m[:, half + h * P:half + (h + 1) * P], MXC[:, p, h, :], ident_r[:],
                                          start=True, stop=True)
                mm.then_inc(max_turned, 1)

            def scores_by_key(b):
                if b >= 2:
                    pe.wait_ge(exp_done, b - 1)
                r = ROWS * (b % 4)
                for h in range(NH):
                    nc.tensor.matmul(bank_st[b % 2][:, h * N:(h + 1) * N], Ks[r:r + ROWS, b // 4, h * P:(h + 1) * P],
                                     Qs[r:r + ROWS, b // 4, :], start=(h == 0), stop=False, skip_group_check=True)
                if b == 0:
                    pe.wait_ge(ones_set, 1)
                pe.wait_ge(max_rows, b // 2 + 1)
                for h in range(NH):
                    mm = nc.tensor.matmul(bank_st[b % 2][:, h * N:(h + 1) * N], neg_ones[r:r + 2, :],
                                          MXT[r:r + 2, b // 2, :], start=False, stop=(h == NH - 1),
                                          skip_group_check=True)
                mm.then_inc(st_ready, 1)

            def weigh_values(p):
                if p == 0:
                    pe.wait_ge(ones_set, 1 + PAIRS)
                if p >= 2:
                    pe.wait_ge(z_done, p - 1)
                for s in range(2):
                    b = 2 * p + s
                    pe.wait_ge(exp_done, b + 1)
                    for h in range(NH):
                        k = (2 * h + s) * P
                        for m in range(NH):
                            mm = nc.tensor.matmul(bank_pv[p % 2][:, k:k + C + 1], E[:, b, m, h * P:(h + 1) * P],
                                                  U[:, p, m, s, 0:C + 1], start=(m == 0), stop=(m == NH - 1))
                mm.then_inc(pv_ready, 1)

            def turn_output(p):
                pe.wait_ge(z_done, p + 1)
                if p >= 1:
                    pe.wait_ge(y_done, p)
                half = (p % 2) * N
                for h in range(NH):
                    mm = nc.tensor.transpose(bank_t[:, half + h * P:half + (h + 1) * P],
                                             Z[:, p, h, :, :].rearrange("p s c -> p (s c)"), ident[:])
                mm.then_inc(turned, 1)

            weights_u()
            group_stats_of(0)
            project_qk(0)
            group_stats_of(1)
            project_u(0)
            scores_by_query(0)
            scores_by_query(1)
            project_qk(1)
            project_u(1)
            for p in range(PAIRS):
                if p + 1 < PAIRS:
                    scores_by_query(2 * p + 2)
                    scores_by_query(2 * p + 3)
                turn_max(p)
                scores_by_key(2 * p)
                if p >= 1:
                    weigh_values(p - 1)
                scores_by_key(2 * p + 1)
                if p >= 1:
                    turn_output(p - 1)
            weigh_values(PAIRS - 1)
            turn_output(PAIRS - 1)


def pack_parameters(norm_w, norm_b, Wq, Wk, Wv, Wproj, gamma, np):
    a = np.zeros((P, A_COLS), np.float32)
    b = np.zeros((P, B_COLS), np.float32)
    part = (np.arange(P) % ROWS) // D
    a[:, A_QMASK] = np.where(part >= 2, -1.0, 0.0)
    a[:, A_KMASK] = np.where(part % 2 == 1, -1.0, 0.0)
    for s in range(2):
        rows = slice(s * C, (s + 1) * C)
        a[rows, A_NORM_W], a[rows, A_NORM_B] = norm_w, norm_b
        for part in range(PARTS):
            k = s * ROWS + part * D
            a[rows, A_WQ + k:A_WQ + k + D] = Wq.T
            a[rows, A_WK + k:A_WK + k + D] = Wk.T
        b[rows, B_WV + s * C:B_WV + (s + 1) * C] = Wv
        b[rows, B_WPROJ + s * C:B_WPROJ + (s + 1) * C] = Wproj.T
    b[:, B_GAMMA] = gamma[0]
    return a, b


def kernel(x, L0_conv_norm_w, L0_conv_norm_b, L0_conv_Wq, L0_conv_Wk, L0_conv_Wv, L0_conv_Wproj, L0_conv_gamma):
    import numpy as np
    import concourse.bacc as bacc
    from concourse.bass_utils import run_bass_kernel_spmd

    x = np.ascontiguousarray(x).reshape(B, C, N)
    a, b = pack_parameters(*(np.asarray(v) for v in (L0_conv_norm_w, L0_conv_norm_b, L0_conv_Wq, L0_conv_Wk,
                                                     L0_conv_Wv, L0_conv_Wproj, L0_conv_gamma)), np)
    nc = bacc.Bacc("TRN2", target_bir_lowering=False, num_devices=1)
    arrays = {"x_dram": x, "pack_a_dram": a, "pack_b_dram": b}
    args = [nc.dram_tensor(name, v.shape, F32, kind="ExternalInput").ap() for name, v in arrays.items()]
    out = nc.dram_tensor("out_dram", (B, C, N), F32, kind="ExternalOutput").ap()
    build_attention(nc, *args, out)
    got = run_bass_kernel_spmd(nc, [arrays], core_ids=[0])
    return got.results[0]["out_dram"].reshape(B, C, HH, WW)
```

```python
from contextlib import ExitStack

import concourse.bass as bass
from concourse import mybir

ALU = mybir.AluOpType
ACT = mybir.ActivationFunctionType
AX_X = mybir.AxisListType.X
F32 = mybir.dt.float32
F32R = mybir.dt.float32r
BF16 = mybir.dt.bfloat16

B, C, HH, WW = 8, 64, 16, 16
N = HH * WW
GROUPS = 32
CPG = C // GROUPS
D = C // 8
EPS = 1e-5
SCALE = float(D) ** -0.5
P = 128
PAIRS = B // 2
QUADS = B // 4
UW = 2 * C
PARTS = 4
ROWS = PARTS * D
NH = N // P

NORM_W, NORM_B, GAMMA, QMASK, KMASK = range(5)
WQ = KMASK + 1
WK = WQ + 2 * ROWS
WV = WK + 2 * ROWS
WPROJ = WV + P
PACK_COLS = WPROJ + P

WARM = (7, 2, 4, 4)


def build_attention(nc, x, pack, out):
    x_pairs = x.rearrange("(j s) c n -> j (s c) n", s=2)
    out_pairs = out.rearrange("(j s) c n -> j (s c) n", s=2)

    with ExitStack() as ctx:
        def sb(name, shape, dt=F32):
            return ctx.enter_context(nc.sbuf_tensor(name, shape, dt))

        def bank(name):
            return ctx.enter_context(nc.psum_tensor(name, [P, 512], F32))

        def sem(name):
            return ctx.enter_context(nc.semaphore(name))

        X = sb("X", [P, PAIRS, N])
        par = sb("par", [P, PACK_COLS])
        zeros = sb("zeros", [P, 512], BF16)
        neg_half_g = sb("neg_half_g", [P, P])
        ident = sb("ident", [P, P])
        ident_r = sb("ident_r", [P, P], F32R)
        neg_ones = sb("neg_ones", [P, P], F32R)
        exponent = sb("exponent", [P, 2])
        warm_exp = sb("warm_exp", [P, 1])
        stats = sb("stats", [P, PAIRS, 6])
        mv = sb("mv", [P, PAIRS, 2])
        dev = sb("dev", [P, PAIRS])
        dev2 = sb("dev2", [P, PAIRS])
        var = sb("var", [P, PAIRS])
        negm_w = sb("negm_w", [P, PAIRS])
        rstd = sb("rstd", [P, PAIRS])
        mul = sb("mul", [P, PAIRS])
        add = sb("add", [P, PAIRS])
        H = sb("H", [P, PAIRS, N])
        WU = sb("WU", [P, P])
        QKhi = sb("QKhi", [P, QUADS, 2 * N], F32R)
        Qs = sb("Qs", [P, QUADS, N], F32R)
        Ks = sb("Ks", [P, QUADS, N], F32R)
        U = sb("U", [P, PAIRS, NH, 2, UW])
        mx = sb("mx", [P, PAIRS, 2, NH])
        MXC = sb("MXC", [P, PAIRS, NH, P], F32R)
        MXT = sb("MXT", [P, PAIRS, N], F32R)
        E = sb("E", [P, B, NH, N])
        rec = sb("rec", [P, PAIRS, NH * 2])
        Z = sb("Z", [P, PAIRS, NH, 2, C])
        Y = sb("Y", [P, PAIRS, N])

        bank_qk = [bank("qk0"), bank("qk1")]
        bank_m = bank("bank_m")
        bank_u = bank("bank_u")
        bank_st = [bank("st0"), bank("st1")]
        bank_s = [bank("s0"), bank("s1")]
        bank_gn = bank_st
        bank_pv = [bank_qk[0], bank_u]
        bank_t = bank_qk[1]

        x_in = [sem(f"x_in{j}") for j in range(PAIRS)]
        par_in = sem("par_in")
        zeros_set, mxc_zeroed, neg_g_set, ident_set = sem("zeros_set"), sem("mxc_zeroed"), sem("neg_g_set"), sem("ident_set")
        exponent_set, identr_set = sem("exponent_set"), sem("identr_set")
        ones_set, pool_chain = sem("ones_set"), sem("pool_chain")
        stats_done, mv_done, group_stats = sem("stats_done"), sem("mv_done"), sem("group_stats")
        dev_done, dev2_done, var_done, negm_w_done = sem("dev_done"), sem("dev2_done"), sem("var_done"), sem("negm_w_done")
        rstd_done, mul_done, add_done = sem("rstd_done"), sem("mul_done"), sem("add_done")
        h_dve, h_act = sem("h_dve"), sem("h_act")
        wu_ready, wu_kept = sem("wu_ready"), sem("wu_kept")
        qk_ready, qk_high, qk_stacked = sem("qk_ready"), sem("qk_high"), sem("qk_stacked")
        u_ready, u_kept = sem("u_ready"), sem("u_kept")
        s_ready, max_done, max_high, max_cols = sem("s_ready"), sem("max_done"), sem("max_high"), sem("max_cols")
        max_turned, max_rows = sem("max_turned"), sem("max_rows")
        st_ready, exp_done = sem("st_ready"), sem("exp_done")
        pv_ready, rec_done, z_done, turned = sem("pv_ready"), sem("rec_done"), sem("z_done"), sem("turned")
        y_done, y_out = sem("y_done"), sem("y_out")

        block = ctx.enter_context(nc.Block())

        @block.sync
        def _(sp):
            for j in (0, 2):
                sp.dma_start(X[:, j, :], x_pairs[j]).then_inc(x_in[j], 16)
            for j in range(PAIRS):
                sp.wait_ge(y_done, j + 1)
                sp.dma_start(out_pairs[j], Y[:, j, :]).then_inc(y_out, 16)
            sp.wait_ge(y_out, 16 * PAIRS)

        @block.gpsimd
        def _(pool):
            nc.gpsimd.memset(ident[:], 0.0).then_inc(pool_chain, 1)
            nc.gpsimd.memset(neg_half_g[:], -1.0 / CPG).then_inc(pool_chain, 1)
            pool.wait_ge(pool_chain, 1)
            nc.gpsimd.affine_select(out=ident[:], in_=ident[:], compare_op=ALU.not_equal, fill=1.0, base=0,
                                    pattern=[[-1, P]], channel_multiplier=1).then_inc(ident_set, 1)
            blocks = neg_half_g[:].rearrange("p (g c) -> p g c", c=CPG)
            pool.wait_ge(pool_chain, 2)
            nc.gpsimd.affine_select(out=blocks, in_=blocks, compare_op=ALU.is_ge, fill=0.0, base=0,
                                    pattern=[[-CPG, P // CPG], [0, CPG]], channel_multiplier=1).then_inc(pool_chain, 1)
            pool.wait_ge(pool_chain, 3)
            nc.gpsimd.affine_select(out=blocks, in_=blocks, compare_op=ALU.is_ge, fill=0.0, base=CPG - 1,
                                    pattern=[[CPG, P // CPG], [0, CPG]], channel_multiplier=-1).then_inc(neg_g_set, 1)
            nc.gpsimd.memset(exponent[:], -0.5).then_inc(exponent_set, 1)
            nc.gpsimd.memset(neg_ones[:].bitcast(F32), -1.0).then_inc(ones_set, 1)
            nc.gpsimd.memset(MXC[:].rearrange("p j h c -> p (j h c)").bitcast(F32), 0.0).then_inc(mxc_zeroed, 1)
            nc.gpsimd.memset(U[:].rearrange("p j h s c -> p (j h s) c")[:, :, C:UW], 1.0).then_inc(ones_set, 1)
            pool.wait_ge(exponent_set, 1)
            for q in range(QUADS):
                two = slice(2 * q, 2 * q + 2)
                pool.wait_ge(var_done, q + 1)
                nc.gpsimd.tensor_tensor(rstd[:, two], var[:, two], exponent[:], ALU.pow).then_inc(rstd_done, 1)

        @block.scalar
        def _(act):
            for j in (1, 3):
                act.dma_start(X[:, j, :], x_pairs[j]).then_inc(x_in[j], 16)
            act.dma_start(par[:], pack).then_inc(par_in, 16)
            act.wait_ge(zeros_set, 1)
            nc.scalar.activation(warm_exp[:], zeros[:, 0:1], ACT.Exp)

            def keep_high(q):
                act.wait_ge(qk_ready, q + 1)
                for t in range(2):
                    cols = slice(t * N, (t + 1) * N)
                    nc.scalar.copy(QKhi[:, q, cols], bank_qk[q][:, cols]).then_inc(qk_high, 1)

            def norm_odd(q):
                j = 2 * q + 1
                act.wait_ge(add_done, 2 * (q + 1))
                act.wait_ge(x_in[j], 16)
                nc.scalar.activation(H[:, j, :], X[:, j, :], ACT.Identity, bias=add[:, j:j + 1],
                                     scale=mul[:, j:j + 1]).then_inc(h_act, 1)

            def keep_u(q):
                act.wait_ge(u_ready, q + 1)
                nc.scalar.copy(U[:, 2 * q:2 * q + 2, :, :, 0:C].rearrange("p j h s c -> p (j h s) c"),
                               bank_u[:].rearrange("p (g c) -> p g c", c=C)).then_inc(u_kept, 1)

            def keep_max_rows(p):
                act.wait_ge(max_turned, p + 1)
                half = (p % 2) * N
                nc.scalar.copy(MXT[:, p, :], bank_m[:, half:half + N]).then_inc(max_rows, 1)

            def exps(b):
                act.wait_ge(st_ready, b + 1)
                nc.scalar.activation(E[:, b, :, :].rearrange("p h n -> p (h n)"), bank_st[b % 2][:], ACT.Exp,
                                     scale=SCALE).then_inc(exp_done, 1)

            def keep_wu():
                act.wait_ge(wu_ready, 1)
                nc.scalar.activation(WU[:], bank_m[:, 0:P], ACT.Copy,
                                     scale=par[:, GAMMA:GAMMA + 1]).then_inc(wu_kept, 1)

            act.wait_ge(ident_set, 1)
            nc.scalar.copy(ident_r[:], ident[:]).then_inc(identr_set, 1)
            norm_odd(0)
            keep_wu()
            norm_odd(1)
            keep_high(0)
            keep_u(0)
            keep_high(1)
            keep_u(1)
            for p in range(PAIRS):
                keep_max_rows(p)
                exps(2 * p)
                exps(2 * p + 1)

        @block.vector
        def _(dve):
            nc.vector.memset(zeros[:], 0.0).then_inc(zeros_set, 1)

            def channel_stats(q):
                for j in (2 * q, 2 * q + 1):
                    dve.wait_ge(x_in[j], 16)
                    nc.vector.bn_stats(stats[:, j, :], X[:, j, :]).then_inc(stats_done, 1)
                for j in (2 * q, 2 * q + 1):
                    dve.wait_ge(stats_done, j + 1)
                    nc.vector.bn_aggr(mv[:, j, :], stats[:, j, :]).then_inc(mv_done, 1)

            def group_var(q):
                two = slice(2 * q, 2 * q + 2)
                dve.wait_ge(group_stats, q + 1)
                neg = bank_gn[q][:, 0:4].rearrange("p (j t) -> p t j", t=2)
                nc.vector.tensor_tensor(dev[:, two], neg[:, 0, :], mv[:, two, 0], ALU.add).then_inc(dev_done, 1)
                dve.wait_ge(dev_done, q + 1)
                nc.vector.tensor_tensor(dev2[:, two], dev[:, two], dev[:, two], ALU.mult).then_inc(dev2_done, 1)
                dve.wait_ge(dev2_done, q + 1)
                nc.vector.scalar_tensor_tensor(out=var[:, two], in0=dev2[:, two], scalar=EPS, in1=neg[:, 1, :],
                                               op0=ALU.add, op1=ALU.subtract).then_inc(var_done, 1)
                if q == 0:
                    dve.wait_ge(par_in, 16)
                nc.vector.tensor_scalar(negm_w[:, two], neg[:, 0, :], par[:, NORM_W:NORM_W + 1], None,
                                        ALU.mult).then_inc(negm_w_done, 1)

            def affine(q):
                j = 2 * q
                dve.wait_ge(rstd_done, q + 1)
                nc.vector.tensor_scalar(mul[:, j:j + 2], rstd[:, j:j + 2], par[:, NORM_W:NORM_W + 1], None,
                                        ALU.mult).then_inc(mul_done, 1)
                dve.wait_ge(negm_w_done, q + 1)
                for i in range(2):
                    nc.vector.tensor_scalar(add[:, j + i:j + i + 1], negm_w[:, j + i:j + i + 1],
                                            rstd[:, j + i:j + i + 1], par[:, NORM_B:NORM_B + 1], ALU.mult,
                                            ALU.add).then_inc(add_done, 1)
                dve.wait_ge(mul_done, q + 1)
                dve.wait_ge(add_done, 2 * q + 1)
                nc.vector.tensor_scalar(H[:, j, :], X[:, j, :], mul[:, j:j + 1], add[:, j:j + 1], ALU.mult,
                                        ALU.add).then_inc(h_dve, 1)

            def stack(q):
                for t, (dst, mask) in enumerate(((Qs, QMASK), (Ks, KMASK))):
                    dve.wait_ge(qk_high, 2 * q + 2)
                    cols = slice(t * N, (t + 1) * N)
                    nc.vector.scalar_tensor_tensor(out=dst[:, q, :], in0=QKhi[:, q, cols].bitcast(F32),
                                                   scalar=par[:, mask:mask + 1], in1=bank_qk[q][:, cols],
                                                   op0=ALU.mult, op1=ALU.add).then_inc(qk_stacked, 1)

            def row_max(b):
                dve.wait_ge(s_ready, b + 1)
                nc.vector.tensor_reduce(mx[:, b // 2, b % 2, :], bank_s[b % 2][:].rearrange("p (h m) -> p h m", h=NH),
                                        AX_X, ALU.max).then_inc(max_done, 1)

            def split_max(p):
                r = 2 * ROWS * (p % 2)
                high = MXC[:, p, :, r:r + ROWS + 1:ROWS].rearrange("p h s -> p s h")
                low = MXC[:, p, :, r + 1:r + ROWS + 2:ROWS].rearrange("p h s -> p s h")
                if p == 0:
                    dve.wait_ge(mxc_zeroed, 1)
                dve.wait_ge(max_done, 2 * p + 2)
                nc.vector.tensor_copy(high, mx[:, p, :, :]).then_inc(max_high, 1)
                dve.wait_ge(max_high, p + 1)
                nc.vector.tensor_tensor(low, mx[:, p, :, :], high.bitcast(F32), ALU.subtract).then_inc(max_cols, 1)

            def normalize(p):
                dve.wait_ge(pv_ready, p + 1)
                pv = bank_pv[p % 2][:].rearrange("p (g c) -> p g c", c=P)
                nc.vector.reciprocal(rec[:, p, :].unsqueeze(2), pv[:, :, C:C + 1]).then_inc(rec_done, 1)
                dve.wait_ge(rec_done, p + 1)
                nc.vector.tensor_tensor(Z[:, p, :, :, :].rearrange("p h s c -> p (h s) c"), pv[:, :, 0:C],
                                        rec[:, p, :].unsqueeze(2).to_broadcast([P, NH * 2, C]),
                                        ALU.mult).then_inc(z_done, 1)

            def residual(p):
                dve.wait_ge(turned, p + 1)
                half = (p % 2) * N
                nc.vector.tensor_tensor(Y[:, p, :], bank_t[:, half:half + N], X[:, p, :], ALU.add).then_inc(y_done, 1)

            channel_stats(0)
            channel_stats(1)
            group_var(0)
            group_var(1)
            affine(0)
            affine(1)
            stack(0)
            row_max(0)
            row_max(1)
            split_max(0)
            stack(1)
            for p in range(1, PAIRS):
                row_max(2 * p)
                row_max(2 * p + 1)
                split_max(p)
                if p == PAIRS - 1:
                    normalize(0)
            for p in range(PAIRS):
                if p > 0:
                    normalize(p)
                residual(p)

        @block.tensor
        def _(pe):
            pe.wait_ge(zeros_set, 1)

            def keep_warm(n):
                for _ in range(n):
                    nc.tensor.matmul(bank_s[0][:], zeros[:, 0:P], zeros[:], start=True, stop=True)

            def weights_u():
                pe.wait_ge(par_in, 16)
                nc.tensor.matmul(bank_m[:, 0:P], par[:, WV:WV + P], par[:, WPROJ:WPROJ + P], start=True,
                                 stop=True).then_inc(wu_ready, 1)

            def group_stats_of(q):
                if q == 0:
                    pe.wait_ge(neg_g_set, 1)
                pe.wait_ge(mv_done, 2 * q + 2)
                nc.tensor.matmul(bank_gn[q][:, 0:4], neg_half_g[:],
                                 mv[:, 2 * q:2 * q + 2, :].rearrange("p j t -> p (j t)"), start=True,
                                 stop=True).then_inc(group_stats, 1)

            def project_qk(q):
                if q == 0:
                    pe.wait_ge(par_in, 16)
                pe.wait_ge(h_dve, q + 1)
                pe.wait_ge(h_act, q + 1)
                for t, w in enumerate((WQ, WK)):
                    for i, j in enumerate((2 * q, 2 * q + 1)):
                        mm = nc.tensor.matmul(bank_qk[q][2 * ROWS * i:2 * ROWS * (i + 1), t * N:(t + 1) * N],
                                              par[:, w:w + 2 * ROWS], H[:, j, :], start=True, stop=True)
                mm.then_inc(qk_ready, 1)

            def project_u(q):
                if q == 0:
                    pe.wait_ge(wu_kept, 1)
                else:
                    pe.wait_ge(u_kept, q)
                for i, j in enumerate((2 * q, 2 * q + 1)):
                    for h in range(NH):
                        k = (i * NH + h) * P
                        mm = nc.tensor.matmul(bank_u[:, k:k + P], H[:, j, h * P:(h + 1) * P], WU[:], start=True,
                                              stop=True)
                mm.then_inc(u_ready, 1)

            def scores_by_query(p):
                if p % 2 == 0:
                    pe.wait_ge(qk_stacked, p + 2)
                if p >= 1:
                    pe.wait_ge(max_done, 2 * p)
                for h in range(NH):
                    for b in (2 * p, 2 * p + 1):
                        r = ROWS * (b % 4)
                        mm = nc.tensor.matmul(bank_s[b % 2][:, h * N:(h + 1) * N],
                                              Qs[r:r + ROWS, b // 4, h * P:(h + 1) * P], Ks[r:r + ROWS, b // 4, :],
                                              start=True, stop=True)
                        if h == NH - 1:
                            mm.then_inc(s_ready, 1)

            def turn_max(p):
                if p == 0:
                    pe.wait_ge(identr_set, 1)
                else:
                    pe.wait_ge(max_rows, p)
                pe.wait_ge(max_cols, p + 1)
                half = (p % 2) * N
                for h in range(NH):
                    mm = nc.tensor.matmul(bank_m[:, half + h * P:half + (h + 1) * P], MXC[:, p, h, :], ident_r[:],
                                          start=True, stop=True)
                mm.then_inc(max_turned, 1)

            def scores_by_key(p):
                if p >= 1:
                    pe.wait_ge(exp_done, 2 * p)
                for h in range(NH):
                    for b in (2 * p, 2 * p + 1):
                        r = ROWS * (b % 4)
                        nc.tensor.matmul(bank_st[b % 2][:, h * N:(h + 1) * N], Ks[r:r + ROWS, b // 4, h * P:(h + 1) * P],
                                         Qs[r:r + ROWS, b // 4, :], start=(h == 0), stop=False, skip_group_check=True)
                if p == 0:
                    pe.wait_ge(ones_set, 1)
                pe.wait_ge(max_rows, p + 1)
                for h in range(NH):
                    for b in (2 * p, 2 * p + 1):
                        r = ROWS * (b % 4)
                        mm = nc.tensor.matmul(bank_st[b % 2][:, h * N:(h + 1) * N], neg_ones[r:r + 2, :],
                                              MXT[r:r + 2, p, :], start=False, stop=(h == NH - 1),
                                              skip_group_check=True)
                        if h == NH - 1:
                            mm.then_inc(st_ready, 1)

            def weigh_values(p, s):
                if p == 0:
                    pe.wait_ge(ones_set, 2)
                if p % 2 == 0:
                    pe.wait_ge(u_kept, p // 2 + 1)
                if p >= 2:
                    pe.wait_ge(z_done, p - 1)
                b = 2 * p + s
                pe.wait_ge(exp_done, b + 1)
                for h in range(NH):
                    k = (2 * h + s) * P
                    for m in range(NH):
                        mm = nc.tensor.matmul(bank_pv[p % 2][:, k:k + UW], E[:, b, m, h * P:(h + 1) * P],
                                              U[:, p, m, s, :], start=(m == 0), stop=(m == NH - 1))
                if s == 1:
                    mm.then_inc(pv_ready, 1)

            def turn_output(p):
                pe.wait_ge(z_done, p + 1)
                if p >= 1:
                    pe.wait_ge(y_done, p)
                half = (p % 2) * N
                for h in range(NH):
                    mm = nc.tensor.transpose(bank_t[:, half + h * P:half + (h + 1) * P],
                                             Z[:, p, h, :, :].rearrange("p s c -> p (s c)"), ident[:])
                mm.then_inc(turned, 1)

            keep_warm(WARM[0])
            group_stats_of(0)
            keep_warm(WARM[1])
            group_stats_of(1)
            weights_u()
            keep_warm(WARM[2])
            project_qk(0)
            project_u(0)
            project_qk(1)
            keep_warm(WARM[3])
            scores_by_query(0)
            project_u(1)
            turn_max(0)
            scores_by_query(1)
            scores_by_key(0)
            turn_max(1)
            scores_by_query(2)
            for p in range(PAIRS):
                weigh_values(p, 0)
                if p + 1 < PAIRS:
                    scores_by_key(p + 1)
                if p >= 1:
                    turn_output(p - 1)
                weigh_values(p, 1)
                if p + 3 < PAIRS:
                    scores_by_query(p + 3)
                if p + 2 < PAIRS:
                    turn_max(p + 2)
            turn_output(PAIRS - 1)


def pack_parameters(norm_w, norm_b, Wq, Wk, Wv, Wproj, gamma, np):
    pack = np.zeros((P, PACK_COLS), np.float32)
    part = (np.arange(P) % ROWS) // D
    pack[:, QMASK] = np.where(part >= 2, -1.0, 0.0)
    pack[:, KMASK] = np.where(part % 2 == 1, -1.0, 0.0)
    for s in range(2):
        rows = slice(s * C, (s + 1) * C)
        pack[rows, NORM_W], pack[rows, NORM_B] = norm_w, norm_b
        for part in range(PARTS):
            k = s * ROWS + part * D
            pack[rows, WQ + k:WQ + k + D] = Wq.T
            pack[rows, WK + k:WK + k + D] = Wk.T
        pack[rows, WV + s * C:WV + (s + 1) * C] = Wv
        pack[rows, WPROJ + s * C:WPROJ + (s + 1) * C] = Wproj.T
    pack[:, GAMMA] = gamma[0]
    return pack


def kernel(x, L0_conv_norm_w, L0_conv_norm_b, L0_conv_Wq, L0_conv_Wk, L0_conv_Wv, L0_conv_Wproj, L0_conv_gamma):
    import numpy as np
    import concourse.bacc as bacc
    from concourse.bass_utils import run_bass_kernel_spmd

    x = np.ascontiguousarray(x).reshape(B, C, N)
    pack = pack_parameters(*(np.asarray(v) for v in (L0_conv_norm_w, L0_conv_norm_b, L0_conv_Wq, L0_conv_Wk,
                                                      L0_conv_Wv, L0_conv_Wproj, L0_conv_gamma)), np)
    nc = bacc.Bacc("TRN2", target_bir_lowering=False, num_devices=1)
    arrays = {"x_dram": x, "pack_dram": pack}
    args = [nc.dram_tensor(name, v.shape, F32, kind="ExternalInput").ap() for name, v in arrays.items()]
    out = nc.dram_tensor("out_dram", (B, C, N), F32, kind="ExternalOutput").ap()
    build_attention(nc, *args, out)
    got = run_bass_kernel_spmd(nc, [arrays], core_ids=[0])
    return got.results[0]["out_dram"].reshape(B, C, HH, WW)
```

```python
from contextlib import ExitStack

import concourse.bass as bass
from concourse import mybir

ALU = mybir.AluOpType
ACT = mybir.ActivationFunctionType
AX_X = mybir.AxisListType.X
F32 = mybir.dt.float32
F32R = mybir.dt.float32r
BF16 = mybir.dt.bfloat16

B, C, HH, WW = 8, 64, 16, 16
N = HH * WW
GROUPS = 32
CPG = C // GROUPS
D = C // 8
EPS = 1e-5
SCALE = float(D) ** -0.5
P = 128
PAIRS = B // 2
QUADS = B // 4
PARTS = 4
ROWS = PARTS * D
NH = N // P

NORM_W, NORM_B, GAMMA, QMASK, KMASK = range(5)
WQ = KMASK + 1
WK = WQ + 2 * ROWS
WV = WK + 2 * ROWS
WPROJ = WV + P
PACK_COLS = WPROJ + P

NORMED_BY_POOL = [(b, NH - 1) for b in range(1, B - 2)]
NORMED_BY_DVE = [(b, h) for b in range(B) for h in range(NH) if (b, h) not in NORMED_BY_POOL]
TURNED_KEPT_BY_DVE = (3,)

WARM = (3968, 768, 896, 384)


def build_attention(nc, x, pack, out):
    x_pairs = x.rearrange("(j s) c n -> j (s c) n", s=2)
    out_pairs = out.rearrange("(j s) c n -> j (s c) n", s=2)

    with ExitStack() as ctx:
        def sb(name, shape, dt=F32):
            return ctx.enter_context(nc.sbuf_tensor(name, shape, dt))

        def bank(name):
            return ctx.enter_context(nc.psum_tensor(name, [P, 512], F32))

        def sem(name):
            return ctx.enter_context(nc.semaphore(name))

        X = sb("X", [P, PAIRS, N])
        par = sb("par", [P, PACK_COLS])
        zeros = sb("zeros", [P, 512], BF16)
        neg_half_g = sb("neg_half_g", [P, P])
        ident = sb("ident", [P, P])
        exponent = sb("exponent", [P, 2])
        warm_exp = sb("warm_exp", [P, 1])
        stats = sb("stats", [P, PAIRS, 6])
        mv = sb("mv", [P, PAIRS, 2])
        dev = sb("dev", [P, PAIRS])
        dev2 = sb("dev2", [P, PAIRS])
        var = sb("var", [P, PAIRS])
        neg_mean = sb("neg_mean", [P, PAIRS])
        rstd = sb("rstd", [P, PAIRS])
        mul = sb("mul", [P, PAIRS])
        XC = sb("XC", [P, PAIRS, N])
        H = sb("H", [P, PAIRS, N])
        WU = sb("WU", [P, P])
        QKhi = sb("QKhi", [P, QUADS, 2 * N], F32R)
        Qs = sb("Qs", [P, QUADS, N], F32R)
        Ks = sb("Ks", [P, QUADS, N], F32R)
        WQS = sb("WQS", [P, 2 * ROWS])
        U = sb("U", [P, PAIRS, NH, P])
        negmax = sb("negmax", [P, B, NH])
        den = sb("den", [P, B, NH])
        rec = sb("rec", [P, B, NH])
        E = sb("E", [P, B, NH, N])
        A = sb("A", [P, B, NH, N])
        AT = sb("AT", [P, B, NH, N])
        Y = sb("Y", [P, PAIRS, N])

        bank_t = [bank("t0"), bank("t1")]
        bank_q, bank_k = bank_t
        bank_s = [bank(f"s{i}") for i in range(4)]
        bank_u = bank("bank_u")
        bank_o = bank("bank_o")
        bank_gn = [bank_s[3], bank_s[2]]
        bank_last = bank_s[0:2]
        last = PAIRS - 1
        outputs = [(p, slice(0, N), (bank_o, bank_u)[p % 2]) for p in range(last)]
        outputs += [(last, slice(0, P), bank_u), (last, slice(P, N), bank_s[2])]

        x_in = [sem(f"x_in{j}") for j in range(PAIRS)]
        par_in = sem("par_in")
        zeros_set, neg_g_set, ident_set = sem("zeros_set"), sem("neg_g_set"), sem("ident_set")
        exponent_set, wq_scaled, pool_chain = sem("exponent_set"), sem("wq_scaled"), sem("pool_chain")
        stats_done, mv_done, group_stats = sem("stats_done"), sem("mv_done"), sem("group_stats")
        dev_done, dev2_done, var_done = sem("dev_done"), sem("dev2_done"), sem("var_done")
        neg_mean_done = sem("neg_mean_done")
        rstd_done, mul_done = sem("rstd_done"), sem("mul_done")
        center_even, center_odd = sem("center_even"), sem("center_odd")
        h_even, h_odd = sem("h_even"), sem("h_odd")
        wu_ready, wu_kept = sem("wu_ready"), sem("wu_kept")
        qk_ready, qk_high, qk_stacked = sem("qk_ready"), [sem("q_high"), sem("k_high")], sem("qk_stacked")
        u_ready, u_kept = sem("u_ready"), sem("u_kept")
        s_ready, max_done, exp_done = sem("s_ready"), sem("max_done"), sem("exp_done")
        rec_done, normed_dve, normed_pool = sem("rec_done"), sem("normed_dve"), sem("normed_pool")
        turned, at_even, at_odd = sem("turned"), sem("at_even"), sem("at_odd")
        at_last, pv_ready = [sem("at_last0"), sem("at_last1")], sem("pv_ready")
        y_done, y_out = sem("y_done"), sem("y_out")

        block = ctx.enter_context(nc.Block())

        @block.sync
        def _(sp):
            for j in (0, 2):
                sp.dma_start(X[:, j, :], x_pairs[j]).then_inc(x_in[j], 16)
            for j in range(last):
                sp.wait_ge(y_done, j + 1)
                sp.dma_start(out_pairs[j], Y[:, j, :]).then_inc(y_out, 16)
            for h in range(NH):
                tokens = slice(h * P, (h + 1) * P)
                sp.wait_ge(y_done, PAIRS + h)
                sp.dma_start(out_pairs[last][:, tokens], Y[:, last, tokens]).then_inc(y_out, 16)
            sp.wait_ge(y_out, 16 * (last + NH))

        @block.gpsimd
        def _(pool):
            nc.gpsimd.memset(ident[:], 0.0).then_inc(pool_chain, 1)
            nc.gpsimd.memset(neg_half_g[:], -1.0 / CPG).then_inc(pool_chain, 1)
            pool.wait_ge(pool_chain, 1)
            nc.gpsimd.affine_select(out=ident[:], in_=ident[:], compare_op=ALU.not_equal, fill=1.0, base=0,
                                    pattern=[[-1, P]], channel_multiplier=1).then_inc(ident_set, 1)
            blocks = neg_half_g[:].rearrange("p (g c) -> p g c", c=CPG)
            pool.wait_ge(pool_chain, 2)
            nc.gpsimd.affine_select(out=blocks, in_=blocks, compare_op=ALU.is_ge, fill=0.0, base=0,
                                    pattern=[[-CPG, P // CPG], [0, CPG]], channel_multiplier=1).then_inc(pool_chain, 1)
            pool.wait_ge(pool_chain, 3)
            nc.gpsimd.affine_select(out=blocks, in_=blocks, compare_op=ALU.is_ge, fill=0.0, base=CPG - 1,
                                    pattern=[[CPG, P // CPG], [0, CPG]], channel_multiplier=-1).then_inc(neg_g_set, 1)
            nc.gpsimd.memset(exponent[:], -0.5).then_inc(exponent_set, 1)
            pool.wait_ge(exponent_set, 1)
            for q in range(QUADS):
                two = slice(2 * q, 2 * q + 2)
                pool.wait_ge(var_done, q + 1)
                nc.gpsimd.tensor_tensor(rstd[:, two], var[:, two], exponent[:], ALU.pow).then_inc(rstd_done, 1)
                if q == 0:
                    pool.wait_ge(par_in, 16)
                    nc.gpsimd.tensor_scalar(WQS[:], par[:, WQ:WQ + 2 * ROWS], SCALE, None,
                                            ALU.mult).then_inc(wq_scaled, 1)
            pool.wait_ge(mul_done, 2)
            pool.wait_ge(center_even, 2)
            nc.gpsimd.tensor_scalar(H[:, 2, :], XC[:, 2, :], mul[:, 2:3], par[:, NORM_B:NORM_B + 1], ALU.mult,
                                    ALU.add).then_inc(h_even, 1)
            for b, h in NORMED_BY_POOL:
                pool.wait_ge(rec_done, b + 1)
                nc.gpsimd.tensor_scalar(A[:, b, h, :], E[:, b, h, :], rec[:, b, h:h + 1], None,
                                        ALU.mult).then_inc(normed_pool, 1)

        @block.scalar
        def _(act):
            for j in (1, 3):
                act.dma_start(X[:, j, :], x_pairs[j]).then_inc(x_in[j], 16)
            act.dma_start(par[:], pack).then_inc(par_in, 16)
            act.wait_ge(zeros_set, 1)
            nc.scalar.activation(warm_exp[:], zeros[:, 0:1], ACT.Exp)

            def keep_high(q, t):
                act.wait_ge(qk_ready, 2 * q + t + 1)
                nc.scalar.copy(QKhi[:, q, t * N:(t + 1) * N], bank_t[t][:, 0:N]).then_inc(qk_high[t], 1)

            def norm_odd(q):
                j = 2 * q + 1
                act.wait_ge(mul_done, q + 1)
                act.wait_ge(center_odd, q + 1)
                act.wait_ge(par_in, 16)
                nc.scalar.activation(H[:, j, :], XC[:, j, :], ACT.Identity, bias=par[:, NORM_B:NORM_B + 1],
                                     scale=mul[:, j:j + 1]).then_inc(h_odd, 1)

            def center(q):
                j = 2 * q + 1
                act.wait_ge(x_in[j], 16)
                act.wait_ge(neg_mean_done, q + 1)
                nc.scalar.activation(XC[:, j, :], X[:, j, :], ACT.Identity,
                                     bias=neg_mean[:, j:j + 1]).then_inc(center_odd, 1)

            def keep_u(q):
                act.wait_ge(u_ready, q + 1)
                nc.scalar.copy(U[:, 2 * q:2 * q + 2, :, :].rearrange("p j h c -> p (j h c)"),
                               bank_u[:]).then_inc(u_kept, 1)

            def exps(b):
                act.wait_ge(max_done, b + 1)
                for h in range(NH):
                    nc.scalar.activation(E[:, b, h, :], bank_s[b % 4][:, h * N:(h + 1) * N], ACT.Exp,
                                         bias=negmax[:, b, h:h + 1], accum_out=den[:, b, h:h + 1]).then_inc(exp_done, 1)

            def keep_turned(b):
                act.wait_ge(turned, b + 1)
                nc.scalar.copy(AT[:, b, :, :].rearrange("p m n -> p (m n)"),
                               bank_t[b % 2][:]).then_inc((at_even, at_odd)[b % 2], 1)

            def keep_wu():
                act.wait_ge(wu_ready, 1)
                nc.scalar.activation(WU[:], bank_o[:, 0:P], ACT.Copy,
                                     scale=par[:, GAMMA:GAMMA + 1]).then_inc(wu_kept, 1)

            center(0)
            keep_wu()
            norm_odd(0)
            center(1)
            keep_high(0, 0)
            keep_high(0, 1)
            norm_odd(1)
            keep_u(0)
            keep_high(1, 0)
            exps(0)
            exps(1)
            keep_u(1)
            for b in range(2, B):
                exps(b)
                if b - 2 not in TURNED_KEPT_BY_DVE:
                    keep_turned(b - 2)
            keep_turned(B - 2)
            act.wait_ge(turned, B)
            nc.scalar.copy(AT[:, B - 1, 0, :], bank_last[0][:, 0:N]).then_inc(at_last[0], 1)

        @block.vector
        def _(dve):
            nc.vector.memset(zeros[:], 0.0).then_inc(zeros_set, 1)

            def channel_stats(j):
                dve.wait_ge(x_in[j], 16)
                nc.vector.bn_stats(stats[:, j, :], X[:, j, :]).then_inc(stats_done, 1)

            def channel_mean_var(j):
                dve.wait_ge(stats_done, j + 1)
                nc.vector.bn_aggr(mv[:, j, :], stats[:, j, :]).then_inc(mv_done, 1)

            def of_quad(q):
                return slice(2 * q, 2 * q + 2), bank_gn[q][:, 0:4].rearrange("p (j t) -> p t j", t=2)

            def group_deviation(q):
                two, neg = of_quad(q)
                dve.wait_ge(group_stats, q + 1)
                nc.vector.tensor_tensor(dev[:, two], neg[:, 0, :], mv[:, two, 0], ALU.add).then_inc(dev_done, 1)
                nc.vector.tensor_copy(neg_mean[:, two], neg[:, 0, :]).then_inc(neg_mean_done, 1)
                dve.wait_ge(dev_done, q + 1)
                nc.vector.tensor_tensor(dev2[:, two], dev[:, two], dev[:, two], ALU.mult).then_inc(dev2_done, 1)

            def group_var(q):
                two, neg = of_quad(q)
                dve.wait_ge(dev2_done, q + 1)
                nc.vector.scalar_tensor_tensor(out=var[:, two], in0=dev2[:, two], scalar=EPS, in1=neg[:, 1, :],
                                               op0=ALU.add, op1=ALU.subtract).then_inc(var_done, 1)

            def center(q):
                j = 2 * q
                dve.wait_ge(neg_mean_done, q + 1)
                nc.vector.tensor_scalar(XC[:, j, :], X[:, j, :], neg_mean[:, j:j + 1], None,
                                        ALU.add).then_inc(center_even, 1)

            def factor(q):
                two = slice(2 * q, 2 * q + 2)
                if q == 0:
                    dve.wait_ge(par_in, 16)
                dve.wait_ge(rstd_done, q + 1)
                nc.vector.tensor_scalar(mul[:, two], rstd[:, two], par[:, NORM_W:NORM_W + 1], None,
                                        ALU.mult).then_inc(mul_done, 1)

            def norm_first():
                dve.wait_ge(center_even, 1)
                dve.wait_ge(mul_done, 1)
                nc.vector.tensor_scalar(H[:, 0, :], XC[:, 0, :], mul[:, 0:1], par[:, NORM_B:NORM_B + 1], ALU.mult,
                                        ALU.add).then_inc(h_even, 1)

            def keep_high(q, t):
                dve.wait_ge(qk_ready, 2 * q + t + 1)
                nc.vector.tensor_copy(QKhi[:, q, t * N:(t + 1) * N], bank_t[t][:, 0:N]).then_inc(qk_high[t], 1)

            def stack(q, t):
                dst, src, mask = ((Qs, bank_q, QMASK), (Ks, bank_k, KMASK))[t]
                dve.wait_ge(qk_high[t], q + 1)
                nc.vector.scalar_tensor_tensor(out=dst[:, q, :], in0=QKhi[:, q, t * N:(t + 1) * N].bitcast(F32),
                                               scalar=par[:, mask:mask + 1], in1=src[:, 0:N],
                                               op0=ALU.mult, op1=ALU.add).then_inc(qk_stacked, 1)

            def row_max(b):
                dve.wait_ge(s_ready, b + 1)
                nc.vector.tensor_reduce(negmax[:, b, :], bank_s[b % 4][:].rearrange("p (h m) -> p h m", h=NH),
                                        AX_X, ALU.max, negate=True).then_inc(max_done, 1)

            def reciprocal(b):
                dve.wait_ge(exp_done, NH * (b + 1))
                nc.vector.reciprocal(rec[:, b, :], den[:, b, :]).then_inc(rec_done, 1)

            def normalize(b):
                dve.wait_ge(rec_done, b + 1)
                for h in range(NH):
                    if (b, h) not in NORMED_BY_POOL:
                        nc.vector.tensor_scalar(A[:, b, h, :], E[:, b, h, :], rec[:, b, h:h + 1], None,
                                                ALU.mult).then_inc(normed_dve, 1)

            def keep_turned(b):
                dve.wait_ge(turned, b + 1)
                nc.vector.tensor_copy(AT[:, b, :, :].rearrange("p m n -> p (m n)"),
                                      bank_t[b % 2][:]).then_inc((at_even, at_odd)[b % 2], 1)

            def keep_last_turned(m):
                dve.wait_ge(turned, B)
                nc.vector.tensor_copy(AT[:, B - 1, m, :], bank_last[m][:, 0:N]).then_inc(at_last[m], 1)

            def residual(n):
                p, tokens, bank = outputs[n]
                dve.wait_ge(pv_ready, n + 1)
                nc.vector.tensor_tensor(Y[:, p, tokens], bank[:, tokens], X[:, p, tokens],
                                        ALU.add).then_inc(y_done, 1)

            channel_stats(0)
            channel_stats(1)
            channel_mean_var(0)
            channel_mean_var(1)
            channel_stats(2)
            group_deviation(0)
            group_var(0)
            center(0)
            channel_stats(3)
            channel_mean_var(2)
            channel_mean_var(3)
            factor(0)
            norm_first()
            group_deviation(1)
            group_var(1)
            center(1)
            factor(1)
            stack(0, 0)
            stack(0, 1)
            row_max(0)
            row_max(1)
            keep_high(1, 1)
            stack(1, 0)
            stack(1, 1)
            for b in range(B):
                reciprocal(b)
                if b + 2 < B:
                    row_max(b + 2)
                normalize(b)
                if b - 1 in TURNED_KEPT_BY_DVE:
                    keep_turned(b - 1)
                if b == 5:
                    residual(0)
            residual(last - 2)
            keep_last_turned(1)
            residual(last - 1)
            for h in range(NH):
                residual(last + h)

        @block.tensor
        def _(pe):
            pe.wait_ge(zeros_set, 1)

            def keep_warm(stage, bank):
                left = WARM[stage]
                while left > 0:
                    n = min(left, 512)
                    nc.tensor.matmul(bank[:, 0:n], zeros[:, 0:P], zeros[:, 0:n], start=True, stop=True)
                    left -= n

            def weights_u():
                pe.wait_ge(par_in, 16)
                nc.tensor.matmul(bank_o[:, 0:P], par[:, WV:WV + P], par[:, WPROJ:WPROJ + P], start=True,
                                 stop=True).then_inc(wu_ready, 1)

            def group_stats_of(q):
                if q == 0:
                    pe.wait_ge(neg_g_set, 1)
                pe.wait_ge(mv_done, 2 * q + 2)
                nc.tensor.matmul(bank_gn[q][:, 0:4], neg_half_g[:],
                                 mv[:, 2 * q:2 * q + 2, :].rearrange("p j t -> p (j t)"), start=True,
                                 stop=True).then_inc(group_stats, 1)

            def project_qk(q):
                if q == 0:
                    pe.wait_ge(wq_scaled, 1)
                pe.wait_ge(h_even, q + 1)
                pe.wait_ge(h_odd, q + 1)
                if q >= 1:
                    pe.wait_ge(qk_stacked, 2 * q)
                for dst, w in ((bank_q, WQS[:]), (bank_k, par[:, WK:WK + 2 * ROWS])):
                    for i, j in enumerate((2 * q, 2 * q + 1)):
                        mm = nc.tensor.matmul(dst[2 * ROWS * i:2 * ROWS * (i + 1), 0:N], w, H[:, j, :], start=True,
                                              stop=True)
                    mm.then_inc(qk_ready, 1)

            def project_u(q):
                if q == 0:
                    pe.wait_ge(wu_kept, 1)
                else:
                    pe.wait_ge(u_kept, q)
                for i, j in enumerate((2 * q, 2 * q + 1)):
                    for h in range(NH):
                        k = (i * NH + h) * P
                        mm = nc.tensor.matmul(bank_u[:, k:k + P], H[:, j, h * P:(h + 1) * P], WU[:], start=True,
                                              stop=True)
                mm.then_inc(u_ready, 1)

            def scores_by_query(p):
                if p % 2 == 0:
                    pe.wait_ge(qk_stacked, p + 2)
                for b in (2 * p, 2 * p + 1):
                    if p >= 2:
                        pe.wait_ge(exp_done, NH * (b - 3))
                    r = ROWS * (b % 4)
                    for h in range(NH):
                        mm = nc.tensor.matmul(bank_s[b % 4][:, h * N:(h + 1) * N],
                                              Qs[r:r + ROWS, b // 4, h * P:(h + 1) * P], Ks[r:r + ROWS, b // 4, :],
                                              start=True, stop=True)
                    mm.then_inc(s_ready, 1)

            def turn_attention(b):
                if b == 0:
                    pe.wait_ge(ident_set, 1)
                    pe.wait_ge(qk_stacked, 2 * QUADS)
                if b == B - 1:
                    pe.wait_ge(exp_done, NH * (B - 2))
                elif b >= 2:
                    pe.wait_ge((at_even, at_odd)[b % 2], b // 2)
                for h in range(NH):
                    if (b, h) in NORMED_BY_POOL:
                        pe.wait_ge(normed_pool, NORMED_BY_POOL.index((b, h)) + 1)
                    else:
                        pe.wait_ge(normed_dve, NORMED_BY_DVE.index((b, h)) + 1)
                    for m in range(NH):
                        if b == B - 1:
                            dst = bank_last[m][:, h * P:(h + 1) * P]
                        else:
                            dst = bank_t[b % 2][:, m * N + h * P:m * N + (h + 1) * P]
                        mm = nc.tensor.transpose(dst, A[:, b, h, m * P:(m + 1) * P], ident[:])
                mm.then_inc(turned, 1)

            def weigh_values(n):
                p, tokens, bank = outputs[n]
                pe.wait_ge(at_even, p + 1)
                if p < last:
                    pe.wait_ge(at_odd, p + 1)
                else:
                    for m in range(NH):
                        pe.wait_ge(at_last[m], 1)
                if p % 2 == 0:
                    pe.wait_ge(u_kept, p // 2 + 1)
                if n == 0:
                    pe.wait_ge(wu_kept, 1)
                if n == 1:
                    pe.wait_ge(u_kept, QUADS)
                if n == last + 1:
                    pe.wait_ge(exp_done, NH * (B - 1))
                elif n >= 2:
                    pe.wait_ge(y_done, n - 1)
                for m in range(NH):
                    for i in range(2):
                        mm = nc.tensor.matmul(bank[i * C:(i + 1) * C, tokens], U[:, p, m, i * C:(i + 1) * C],
                                              AT[:, 2 * p + i, m, tokens], start=(m == 0), stop=(m == NH - 1))
                mm.then_inc(pv_ready, 1)

            keep_warm(0, bank_s[0])
            group_stats_of(0)
            keep_warm(1, bank_s[0])
            weights_u()
            keep_warm(2, bank_s[0])
            group_stats_of(1)
            keep_warm(3, bank_s[0])
            project_qk(0)
            project_u(0)
            scores_by_query(0)
            project_qk(1)
            project_u(1)
            scores_by_query(1)
            for p in range(PAIRS):
                if p + 2 < PAIRS:
                    scores_by_query(p + 2)
                turn_attention(2 * p)
                if p == last:
                    turn_attention(2 * p + 1)
                if p >= 1:
                    weigh_values(p - 1)
                if p < last:
                    turn_attention(2 * p + 1)
            for h in range(NH):
                weigh_values(last + h)


def pack_parameters(norm_w, norm_b, Wq, Wk, Wv, Wproj, gamma, np):
    pack = np.zeros((P, PACK_COLS), np.float32)
    part = (np.arange(P) % ROWS) // D
    pack[:, QMASK] = np.where(part >= 2, -1.0, 0.0)
    pack[:, KMASK] = np.where(part % 2 == 1, -1.0, 0.0)
    for s in range(2):
        rows = slice(s * C, (s + 1) * C)
        pack[rows, NORM_W], pack[rows, NORM_B] = norm_w, norm_b
        for part in range(PARTS):
            k = s * ROWS + part * D
            pack[rows, WQ + k:WQ + k + D] = Wq.T
            pack[rows, WK + k:WK + k + D] = Wk.T
        pack[rows, WV + s * C:WV + (s + 1) * C] = Wv
        pack[rows, WPROJ + s * C:WPROJ + (s + 1) * C] = Wproj.T
    pack[:, GAMMA] = gamma[0]
    return pack


def kernel(x, L0_conv_norm_w, L0_conv_norm_b, L0_conv_Wq, L0_conv_Wk, L0_conv_Wv, L0_conv_Wproj, L0_conv_gamma):
    import numpy as np
    import concourse.bacc as bacc
    from concourse.bass_utils import run_bass_kernel_spmd

    x = np.ascontiguousarray(x).reshape(B, C, N)
    pack = pack_parameters(*(np.asarray(v) for v in (L0_conv_norm_w, L0_conv_norm_b, L0_conv_Wq, L0_conv_Wk,
                                                      L0_conv_Wv, L0_conv_Wproj, L0_conv_gamma)), np)
    nc = bacc.Bacc("TRN2", target_bir_lowering=False, num_devices=1)
    arrays = {"x_dram": x, "pack_dram": pack}
    args = [nc.dram_tensor(name, v.shape, F32, kind="ExternalInput").ap() for name, v in arrays.items()]
    out = nc.dram_tensor("out_dram", (B, C, N), F32, kind="ExternalOutput").ap()
    build_attention(nc, *args, out)
    got = run_bass_kernel_spmd(nc, [arrays], core_ids=[0])
    return got.results[0]["out_dram"].reshape(B, C, HH, WW)
```
